# Optimizing a Trainium2 kernel written in Bass

```python
import numpy as np
import jax
import jax.numpy as jnp

def _softmax(x, axis=-1):
    return jax.nn.softmax(x, axis=axis)

def _gelu(x):
    return jax.nn.gelu(x, approximate=True)

def _silu(x):
    return jax.nn.silu(x)

def _sigmoid(x):
    return jax.nn.sigmoid(x)

def _layernorm(x, axis=-1, eps=1e-05):
    m = jnp.mean(x, axis=axis, keepdims=True)
    v = jnp.var(x, axis=axis, keepdims=True)
    return (x - m) / jnp.sqrt(v + eps)

def _scatter_add(tgt, idx, src, axis=0):
    return tgt.at[idx].add(src)

def _segment_sum(src, seg, n):
    return jax.ops.segment_sum(src, seg, n)
kernel_name = 'mk_adj_preln_d1_adj_r2_f6f162'

def setup_inputs(seed: int=0):
    np.random.seed(seed)
    _w = jnp.asarray

    def _rec_inputs():
        import jax
        import jax.numpy as jnp
        _gk = jax.random.key(seed)
        x = 7.22e-05 + 1 * jax.random.normal(jax.random.fold_in(_gk, 1), (1354, 512), jnp.float32)
        _a = jax.random.bernoulli(jax.random.fold_in(_gk, 2), 0.00295421, (1354, 1354))
        _a = jnp.logical_or(_a, jnp.swapaxes(_a, -1, -2))
        _a = jnp.logical_or(_a, jnp.eye(1354, dtype=bool))
        _af = _a.astype(jnp.float32)
        _d = jnp.maximum(_af.sum(-1), 1.0) ** (-0.5)
        _af = _af * _d[..., :, None] * _d[..., None, :]
        adj = _af
        return (x, adj)
    x, adj = _rec_inputs()

    def _L0_gnn_setup():
        import jax, jax.numpy as jnp
        import numpy as np
        N = 4096
        D = 512

        def adjacent_mat(adj):
            adj = adj + jnp.eye(adj.shape[0], dtype=adj.dtype)
            deg = jnp.sum(adj, axis=1)
            dinv = jnp.where(deg > 0, deg ** (-0.5), 0.0).astype(adj.dtype)
            return dinv[:, None] * adj * dinv[None, :]
        key = jax.random.key(seed)
        k1, k2 = jax.random.split(key)
        x = jax.random.normal(k1, (N, D), dtype=jnp.float32)
        Coefficient2 = 1e-08 * jnp.ones((N, N), dtype=jnp.float32)
        A = jax.random.uniform(k2, (N, N), dtype=jnp.float32)
        return {'x': x, 'Coefficient2': Coefficient2, 'A': A}
    _L0_gnn_all = _L0_gnn_setup()
    _L0_gnn_in = {k: v for k, v in _L0_gnn_all.items() if k in ()}
    del _L0_gnn_all
    return {'x': x, 'adj': adj}

def reference(x, adj):
    import jax
    import jax.numpy as jnp

    def _L0_gnn_ref(x, Coefficient2, A):
        import jax, jax.numpy as jnp
        import numpy as np
        N = 4096
        D = 512

        def adjacent_mat(adj):
            adj = adj + jnp.eye(adj.shape[0], dtype=adj.dtype)
            deg = jnp.sum(adj, axis=1)
            dinv = jnp.where(deg > 0, deg ** (-0.5), 0.0).astype(adj.dtype)
            return dinv[:, None] * adj * dinv[None, :]
        A_c = jax.lax.stop_gradient(A)
        adj = adjacent_mat((A_c + A_c.T) * 0.5)
        y = Coefficient2 @ adj
        y = y @ x
        return y
    h = jnp.maximum(_layernorm(x, axis=-1), 0.0)
    x = x + _L0_gnn_ref(h, adj, adj)
    return x

_drawn_inputs = setup_inputs


def setup_inputs(seed=0):
    import zlib

    import numpy as np

    out = dict(_drawn_inputs(seed))
    spreads = {}
    factors = {}
    for name, (base, spread) in spreads.items():
        noise = np.random.default_rng([zlib.crc32(name.encode()), seed]).standard_normal(out[name].shape)
        drawn = base * np.exp(spread * noise) if base else spread * noise
        out[name] = jnp.asarray(drawn.astype(out[name].dtype))
    for name, factor in factors.items():
        out[name] = (out[name] * factor).astype(out[name].dtype)
    return out
```

```python
import concourse.bass as bass
from concourse import mybir
from contextlib import ExitStack



def graph_layer(nc: bass.Bass, x: bass.AP, A: bass.AP, out: bass.AP):
    f32 = mybir.dt.float32
    f32r = mybir.dt.float32r
    ALU = mybir.AluOpType
    ACT = mybir.ActivationFunctionType

    P = 128
    N, D = x.shape
    NB = -(-N // P)
    TAIL = N - (NB - 1) * P
    T64 = 64
    LO = 6
    HALVES = ((0, LO), (LO, NB))
    NHI = NB - LO
    NSEQ = NHI + NB
    SLOTS = 4
    EPS = 1e-5
    TINY = 1.1754943508222875e-38

    def size(i):
        return TAIL if i == NB - 1 else P

    def end(i):
        return min(i * P, N)

    CUTS = ((0, 4), (4, 6), (6, 9), (9, NB))
    GROUPS = [[(max(a, n), b) for a, b in CUTS if b > n] for n in range(NB)]
    FIRST = [sum(len(g) for g in GROUPS[:n]) for n in range(NB + 1)]
    below = [max(a, n + 1) < b for n in range(NB) for a, b in GROUPS[n]]
    BELOW = [sum(below[:q]) for q in range(len(below) + 1)]
    EARLY = FIRST[2]
    PLACES = {4: (0, 2, 3, 5), 3: (0, 2, 4), 2: (1, 3), 1: (1,)}

    def chunk(s, half):
        return NB + 2 * s + half

    ctx = ExitStack()
    with ctx:
        def sb(name, shape, dt):
            return ctx.enter_context(nc.sbuf_tensor(name, shape, dt))

        def sem(name):
            return ctx.enter_context(nc.semaphore(name))

        def next_offset():
            return -(-nc.sbuf_base // 32) * 32

        def at(name, shape, dt, offset):
            return nc.alloc_sbuf_tensor_at(name, shape, dt, offset=offset)

        z_at = next_offset()
        sb("zone_z", [P, NB * 2 * D], f32)
        g_at = next_offset()
        sb("zone_g", [P, NB * 2 * D], f32)

        lo_bytes = NB * LO * P * 4
        A_lo = at("A_lo", [P, NB, LO * P], f32, z_at)
        x_in = at("x_in", [P, 3, D], f32, z_at + lo_bytes)
        xr = at("xr", [P, 2, D], f32, z_at + lo_bytes + 3 * D * 4)
        z = at("z", [P, NB, 2, D], f32r, z_at)
        g = at("g", [P, NB, 2, D], f32r, g_at)
        x_res = at("x_res", [P, NB, D], f32, g_at)
        y_out = at("y_out", [P, NB, D], f32, g_at + NB * D * 4)

        A_hi = sb("A_hi", [P, NB, N - LO * P], f32)
        AT = sb("AT", [P, NB, N], f32)
        ring = sb("ring", [P, SLOTS, 2, LO * P], f32r)
        ident = sb("ident", [P, P], f32)
        neg_half = sb("neg_half", [P, 2], f32)
        stats = sb("stats", [P, NB, 6], f32)
        moments = sb("moments", [P, NB, 2], f32)
        sums = sb("sums", [P, NB, 2], f32)
        degree = sb("degree", [P, NB], f32)
        positive = sb("positive", [P, NB], f32)
        base = sb("base", [P, NB, 2], f32)
        power = sb("power", [P, NB, 2], f32)
        g_scale = sb("g_scale", [P, NB], f32)
        z_scale = sb("z_scale", [P, NB], f32)

        bank = [ctx.enter_context(nc.psum_tensor(f"bank{b}", [P, D], f32)) for b in range(8)]

        load_done = [sem(f"load_done{n}") for n in range(NB)]
        x_done = [sem(f"x_done{n}") for n in range(NB)]
        res_done = sem("res_done")
        out_done = sem("out_done")
        ident_zero = sem("ident_zero")
        ident_ready = sem("ident_ready")
        exponent_ready = sem("exponent_ready")
        transposed = sem("transposed")
        row_stored = sem("row_stored")
        at_stored = sem("at_stored")
        eye_added = sem("eye_added")
        c_added = sem("c_added")
        r_added = sem("r_added")
        heads = sem("heads")
        rests = sem("rests")
        chunk_used = sem("chunk_used")
        sums_ready = sem("sums_ready")
        stats_ready = sem("stats_ready")
        moments_ready = sem("moments_ready")
        var_ready = sem("var_ready")
        xr_ready = sem("xr_ready")
        degree_ready = sem("degree_ready")
        base_ready = sem("base_ready")
        power_ready = sem("power_ready")
        scale_ready = sem("scale_ready")
        g_head = sem("g_head")
        g_ready = sem("g_ready")
        z_head = sem("z_head")
        drained = sem("drained")

        def S_blocks(rows, i0, i1):
            if i1 <= LO:
                return A_lo[:, rows, i0 * P:end(i1)]
            return A_hi[:, rows, i0 * P - LO * P:end(i1) - LO * P]

        def slots_of(s):
            return [chunk(s, half) % SLOTS for half in range(2)]

        def column(s):
            i = LO + s if s < NHI else s - NHI
            cols = size(i)
            if s < NHI:
                return (lambda ks, r: A_hi[0:r, ks, (i - LO) * P:(i - LO) * P + cols]), cols
            return (lambda ks, r: AT[0:r, ks, i * P:i * P + cols]), cols

        def group_banks(q):
            pair = 3 if q >= EARLY else (q + 3) % 4
            return bank[2 * pair], bank[2 * pair + 1]

        steps = [(n, j, FIRST[n] + j, a, b) for n in range(NB) for j, (a, b) in enumerate(GROUPS[n])]
        NQ = len(steps)

        def groups_of(n):
            return [s for s in steps if s[0] == n]

        load_total = [16 * ((n < NB - 1) + (n < LO) + (n < NB - 2) + 4 * (n == 0)) for n in range(NB)]

        block = ctx.enter_context(nc.Block())

        @block.sync
        def _(sp):
            full = (NB - 1) * P
            for n in range(NB):
                rows = slice(n * P, n * P + size(n))
                if n < NB - 1:
                    if n < LO:
                        sp.dma_start(A_lo[:, n, n * P:], A[rows, n * P:LO * P]).then_inc(load_done[n], 16)
                    c0 = max(n, LO) * P
                    sp.dma_start(A_hi[:, n, c0 - LO * P:], A[rows, c0:]).then_inc(load_done[n], 16)
                if n < NB - 2:
                    sp.dma_start(S_blocks(slice(n + 1, NB - 1), n, n + 1),
                                 A[(n + 1) * P:full, n * P:(n + 1) * P].rearrange("(k p) c -> p k c", p=P)
                                 ).then_inc(load_done[n], 16)
                if n == 0:
                    for p0, p1 in ((0, T64), (T64, TAIL)):
                        sp.dma_start(A_lo[p0:p1, NB - 1, :], A[full + p0:full + p1, 0:LO * P]
                                     ).then_inc(load_done[n], 16)
                        sp.dma_start(A_hi[p0:p1, NB - 1, :], A[full + p0:full + p1, LO * P:]
                                     ).then_inc(load_done[n], 16)
                if n >= 3:
                    sp.wait_ge(xr_ready, n - 2)
                for p0, p1 in ((0, P),) if n < NB - 1 else ((0, T64), (T64, TAIL)):
                    sp.dma_start(x_in[p0:p1, n % 3, :], x[n * P + p0:n * P + p1, :]).then_inc(x_done[n], 16)

            sp.wait_ge(chunk_used, chunk(NHI, 0))
            sp.dma_start(x_res[:, 0:NB - 1, :], x[0:full, :].rearrange("(k p) d -> p k d", p=P)
                         ).then_inc(res_done, 16)
            for p0, p1 in ((0, T64), (T64, TAIL)):
                sp.dma_start(x_res[p0:p1, NB - 1, :], x[full + p0:full + p1, :]).then_inc(res_done, 16)
            with sp.Fori(0, NB - 1) as m:
                sp.wait_ge(drained, 2 + NHI + 1 + m)
                sp.dma_start(out[bass.ds(m * P, P), :], y_out[:, bass.ds(m, 1), :].rearrange("p o d -> p (o d)")
                             ).then_inc(out_done, 16)
            sp.wait_ge(drained, 2 + NSEQ)
            for p0, p1 in ((0, T64), (T64, TAIL)):
                sp.dma_start(out[full + p0:full + p1, :], y_out[p0:p1, NB - 1, :]).then_inc(out_done, 16)
            sp.wait_ge(out_done, (NB + 1) * 16)

        @block.gpsimd
        def _(pool):
            nc.gpsimd.memset(ident[:], 0.0).then_inc(ident_zero, 1)
            nc.gpsimd.memset(neg_half[:], -0.5).then_inc(exponent_ready, 1)
            pool.wait_ge(ident_zero, 1)
            nc.gpsimd.affine_select(out=ident[:], in_=ident[:], compare_op=ALU.not_equal, fill=1.0, base=0,
                                    pattern=[[-1, P]], channel_multiplier=1).then_inc(ident_ready, 1)
            pool.wait_ge(exponent_ready, 1)

            def add_columns(n):
                for _, _, q, a, b in groups_of(n):
                    a = max(a, n + 1)
                    if a >= b:
                        continue
                    pool.wait_ge(at_stored, BELOW[q + 1])
                    parts = []
                    if b > a and min(b, NB - 1) > a:
                        parts.append((P, slice(a, min(b, NB - 1))))
                    if b == NB:
                        parts.append((TAIL, slice(NB - 1, NB)))
                    for r, ks in parts:
                        blocks = S_blocks(ks, n, n + 1)[0:r]
                        last = nc.gpsimd.tensor_tensor(blocks, blocks, AT[0:r, ks, n * P:(n + 1) * P], ALU.add)
                    last.then_inc(r_added, 1)

            def powers(n):
                r = size(n)
                pool.wait_ge(var_ready, n + 1)
                pool.wait_ge(base_ready, n + 1)
                nc.gpsimd.tensor_tensor(power[0:r, n, :], base[0:r, n, :], neg_half[0:r, :],
                                        ALU.pow).then_inc(power_ready, 1)

            add_columns(0)
            powers(0)
            add_columns(1)
            for n in range(1, NB):
                powers(n)
                if n + 1 < NB:
                    add_columns(n + 1)

        @block.scalar
        def _(act):
            def store_group(n, q, a, b):
                act.wait_ge(transposed, q + 1)
                row_bank, col_bank = group_banks(q)
                nc.scalar.copy(AT[0:size(n), n, a * P:end(b)],
                               row_bank[0:size(n), 0:end(b) - a * P]).then_inc(row_stored, 1)
                a2, full_end = max(a, n + 1), min(b, NB - 1)
                if a2 < b:
                    blocks = col_bank[:, :].rearrange("p (k c) -> p k c", c=P)
                    if full_end > a2:
                        last = nc.scalar.copy(AT[:, a2:full_end, n * P:(n + 1) * P],
                                              blocks[:, a2 - a:full_end - a, :])
                    if b == NB:
                        last = nc.scalar.copy(AT[0:TAIL, NB - 1, n * P:(n + 1) * P], blocks[0:TAIL, NB - 1 - a, :])
                    last.then_inc(at_stored, 1)

            def head_lo(n):
                r = size(n)
                act.wait_ge(c_added, FIRST[n + 1])
                if n > 0:
                    act.wait_ge(r_added, BELOW[FIRST[n]])
                if n >= SLOTS:
                    act.wait_ge(chunk_used, n - SLOTS + 1)
                nc.scalar.activation(ring[0:r, n % SLOTS, 0, :], A_lo[0:r, n, :], ACT.Copy,
                                     accum_out=sums[0:r, n, 0:1]).then_inc(heads, 1)
                nc.scalar.activation(A_hi[0:r, n, :], A_hi[0:r, n, :], ACT.Copy,
                                     accum_out=sums[0:r, n, 1:2]).then_inc(sums_ready, 1)

            for n in (0, 1):
                for _, _, q, a, b in groups_of(n):
                    store_group(n, q, a, b)
                if n == 0:
                    head_lo(0)
            for n in range(1, NB):
                head_lo(n)
                if n + 1 < NB:
                    for _, _, q, a, b in groups_of(n + 1):
                        store_group(n + 1, q, a, b)

            def head_column(c, slots, source, cols):
                for half, (k0, k1) in enumerate(HALVES):
                    act.wait_ge(chunk_used, c + half - SLOTS + 1)
                    v = ring[:, slots[half], 0, 0:(k1 - k0) * P].rearrange("p (k c) -> p k c", c=P)
                    kf = min(k1, NB - 1)
                    last = nc.scalar.copy(v[:, 0:kf - k0, 0:cols], source(slice(k0, kf), P))
                    if k1 == NB:
                        last = nc.scalar.copy(v[0:TAIL, kf - k0, 0:cols], source(kf, TAIL))
                    last.then_inc(heads, 1)

            def head_of(s):
                head_column(chunk(s, 0), slots_of(s), *column(s))

            act.wait_ge(sums_ready, NB)
            for s in (0, 1):
                head_of(s)

            def z_evac(i, src):
                r = size(i)
                nc.scalar.activation(z[0:r, i, 0, :], src[0:r, :], ACT.Copy,
                                     scale=z_scale[0:r, i:i + 1]).then_inc(z_head, 1)

            act.wait_ge(chunk_used, NB)
            act.wait_ge(rests, NB)
            act.wait_ge(g_ready, NB)
            for i in range(LO):
                z_evac(i, bank[i])
            for s in range(2, 2 + NHI):
                head_of(s)
                act.wait_ge(chunk_used, chunk(s - 2, 2))
                z_evac(LO + s - 2, bank[6 + (s - 2) % 2])
            with act.Fori(0, (NSEQ - 1 - (2 + NHI)) // 2) as it:
                for odd in range(2):
                    s0 = 2 + NHI + odd
                    head_column(chunk(s0, 0) + 4 * it, slots_of(s0),
                                lambda ks, r: AT[0:r, ks, bass.ds((s0 - NHI + 2 * it) * P, P)], P)
            head_of(NSEQ - 1)

        @block.vector
        def _(dve):
            def normalise(n):
                r = size(n)
                dve.wait_ge(x_done[n], 16 if n < NB - 1 else 32)
                nc.vector.bn_stats(stats[0:r, n, :], x_in[0:r, n % 3, :]).then_inc(stats_ready, 1)
                dve.wait_ge(stats_ready, n + 1)
                nc.vector.bn_aggr(moments[0:r, n, :], stats[0:r, n, :]).then_inc(moments_ready, 1)
                dve.wait_ge(moments_ready, n + 1)
                nc.vector.tensor_scalar(base[0:r, n, 0:1], moments[0:r, n, 1:2], EPS, None,
                                        ALU.add).then_inc(var_ready, 1)
                nc.vector.tensor_scalar(xr[0:r, n % 2, :], x_in[0:r, n % 3, :], moments[0:r, n, 0:1], 0.0,
                                        ALU.subtract, ALU.max).then_inc(xr_ready, 1)

            def add_group(n, q, a, b):
                r = size(n)
                dve.wait_ge(row_stored, q + 1)
                if a == n:
                    diag = S_blocks(n, n, n + 1)[0:r]
                    nc.vector.scalar_tensor_tensor(out=diag, in0=ident[0:r, 0:r], scalar=2.0, in1=diag,
                                                   op0=ALU.mult, op1=ALU.add).then_inc(eye_added, 1)
                    dve.wait_ge(eye_added, n + 1)
                blocks = S_blocks(n, a, b)[0:r]
                nc.vector.tensor_tensor(blocks, blocks, AT[0:r, n, a * P:end(b)],
                                        ALU.add).then_inc(c_added, 1)

            def degrees(n):
                r = size(n)
                dve.wait_ge(sums_ready, n + 1)
                nc.vector.tensor_scalar(degree[0:r, n:n + 1], sums[0:r, n, 0:1], sums[0:r, n, 1:2], 0.5,
                                        ALU.add, ALU.mult).then_inc(degree_ready, 1)
                dve.wait_ge(degree_ready, n + 1)
                nc.vector.tensor_scalar(positive[0:r, n:n + 1], degree[0:r, n:n + 1], 0.0, None, ALU.is_gt)
                nc.vector.tensor_scalar(base[0:r, n, 1:2], degree[0:r, n:n + 1], TINY, None,
                                        ALU.max).then_inc(base_ready, 1)

            def rest_lo(n):
                r = size(n)
                dve.wait_ge(heads, n + 1)
                nc.vector.tensor_tensor(ring[0:r, n % SLOTS, 1, :], A_lo[0:r, n, :],
                                        ring[0:r, n % SLOTS, 0, :].bitcast(f32), ALU.subtract).then_inc(rests, 1)

            def make_g(n):
                r = size(n)
                dve.wait_ge(power_ready, n + 1)
                dve.wait_ge(base_ready, n + 1)
                nc.vector.tensor_scalar(z_scale[0:r, n:n + 1], power[0:r, n, 1:2], positive[0:r, n:n + 1], 0.5,
                                        ALU.mult, ALU.mult)
                nc.vector.tensor_scalar(g_scale[0:r, n:n + 1], power[0:r, n, 1:2], positive[0:r, n:n + 1],
                                        power[0:r, n, 0:1], ALU.mult, ALU.mult).then_inc(scale_ready, 1)
                dve.wait_ge(scale_ready, n + 1)
                dve.wait_ge(xr_ready, n + 1)
                nc.vector.tensor_scalar(g[0:r, n, 0, :], xr[0:r, n % 2, :], g_scale[0:r, n:n + 1], None,
                                        ALU.mult).then_inc(g_head, 1)
                dve.wait_ge(g_head, n + 1)
                nc.vector.scalar_tensor_tensor(out=g[0:r, n, 1, :], in0=xr[0:r, n % 2, :],
                                               scalar=g_scale[0:r, n:n + 1], in1=g[0:r, n, 0, :].bitcast(f32),
                                               op0=ALU.mult, op1=ALU.subtract).then_inc(g_ready, 1)

            dve.wait_ge(ident_ready, 1)
            normalise(0)
            for _, _, q, a, b in groups_of(0):
                add_group(0, q, a, b)
            for _, _, q, a, b in groups_of(1)[0:1]:
                add_group(1, q, a, b)
            degrees(0)
            rest_lo(0)
            make_g(0)
            for _, _, q, a, b in groups_of(1)[1:]:
                add_group(1, q, a, b)
            normalise(1)
            for n in range(1, NB):
                todo = groups_of(n + 1) if n + 1 < NB else []
                degrees(n)
                for _, _, q, a, b in todo[0:1]:
                    add_group(n + 1, q, a, b)
                rest_lo(n)
                for _, _, q, a, b in todo[1:2]:
                    add_group(n + 1, q, a, b)
                make_g(n)
                for _, _, q, a, b in todo[2:]:
                    add_group(n + 1, q, a, b)
                if n + 1 < NB:
                    normalise(n + 1)

            dve.sem_inc(drained, 2)

            def rest_column(c, slots, source, cols):
                for half, (k0, k1) in enumerate(HALVES):
                    dve.wait_ge(heads, c + half + 1)
                    v = ring[:, slots[half], :, 0:(k1 - k0) * P].rearrange("p t (k c) -> p t k c", c=P)
                    kf = min(k1, NB - 1)
                    last = nc.vector.tensor_tensor(v[:, 1, 0:kf - k0, 0:cols], source(slice(k0, kf), P),
                                                   v[:, 0, 0:kf - k0, 0:cols].bitcast(f32), ALU.subtract)
                    if k1 == NB:
                        last = nc.vector.tensor_tensor(v[0:TAIL, 1, kf - k0, 0:cols], source(kf, TAIL),
                                                       v[0:TAIL, 0, kf - k0, 0:cols].bitcast(f32), ALU.subtract)
                    last.then_inc(rests, 1)

            def rest_of(s):
                rest_column(chunk(s, 0), slots_of(s), *column(s))

            def z_rest(i, src):
                r = size(i)
                dve.wait_ge(z_head, i + 1)
                last = nc.vector.scalar_tensor_tensor(out=z[0:r, i, 1, :], in0=src[0:r, :],
                                                      scalar=z_scale[0:r, i:i + 1],
                                                      in1=z[0:r, i, 0, :].bitcast(f32),
                                                      op0=ALU.mult, op1=ALU.subtract)
                return last

            for s in (0, 1):
                rest_of(s)
            for i in range(LO):
                z_rest(i, bank[i])
            for s in range(2, 2 + NHI):
                rest_of(s)
                z_rest(LO + s - 2, bank[6 + (s - 2) % 2]).then_inc(drained, 1)
            dve.wait_ge(res_done, 48)

            def result(m, slot, r=P):
                dst = y_out[0:r, bass.ds(m, 1), :].rearrange("p o d -> p (o d)")
                res = x_res[0:r, bass.ds(m, 1), :].rearrange("p o d -> p (o d)")
                nc.vector.tensor_tensor(dst, bank[slot][0:r, :], res,
                                        ALU.add).then_inc(drained, 1)

            with dve.Fori(0, (NSEQ - 1 - (2 + NHI)) // 2) as it:
                for odd in range(2):
                    s0 = 2 + NHI + odd
                    rest_column(chunk(s0, 0) + 4 * it, slots_of(s0),
                                lambda ks, r: AT[0:r, ks, bass.ds((s0 - NHI + 2 * it) * P, P)], P)
                    dve.wait_ge(chunk_used, chunk(s0 - 2, 2) + 4 * it)
                    result(odd + 2 * it, 6 + (s0 - 2) % 2)
            rest_of(NSEQ - 1)
            for s in range(NSEQ - 3, NSEQ):
                dve.wait_ge(chunk_used, chunk(s, 2))
                result(s - NHI, 6 + s % 2, size(s - NHI))

        @block.tensor
        def _(pe):
            def groups_stored(q):
                pe.wait_ge(row_stored, q)
                pe.wait_ge(at_stored, BELOW[q])

            def transpose_group(n, q, a, b):
                if q < EARLY:
                    if q >= 4:
                        groups_stored(q - 3)
                else:
                    groups_stored(q)
                row_bank, col_bank = group_banks(q)
                r = size(n)
                for i in range(a, b):
                    o = (i - a) * P
                    last = nc.tensor.transpose(row_bank[0:r, o:o + size(i)], S_blocks(i, n, n + 1)[0:size(i)],
                                               ident[0:size(i), 0:size(i)])
                    if i > n:
                        last = nc.tensor.transpose(col_bank[0:size(i), o:o + r], S_blocks(n, i, i + 1)[0:r],
                                                   ident[0:r, 0:r])
                last.then_inc(transposed, 1)

            def three(dst, c, b, m, rhs, first, final, r):
                head = ring[0:r, c, 0, b * P:b * P + m]
                rest = ring[0:r, c, 1, b * P:b * P + m]
                nc.tensor.matmul(dst, head, rhs[0:r, 0, :], start=first, stop=False)
                nc.tensor.matmul(dst, head, rhs[0:r, 1, :], start=False, stop=False)
                return nc.tensor.matmul(dst, rest, rhs[0:r, 0, :], start=False, stop=final)

            pe.wait_ge(ident_ready, 1)
            for n in (0, 1):
                pe.wait_ge(load_done[n], load_total[n])
                for _, _, q, a, b in groups_of(n):
                    transpose_group(n, q, a, b)

            groups_stored(EARLY)
            for k in range(NB):
                todo = groups_of(k + 2) if k + 2 < NB else []
                places = PLACES[len(todo)] if todo else ()
                pe.wait_ge(rests, k + 1)
                pe.wait_ge(g_ready, k + 1)
                for i in range(LO):
                    last = three(bank[i][:, :], k % SLOTS, i, P, g[:, k], k == 0, k == NB - 1, size(k))
                    if i in places:
                        if i == places[0] and load_total[k + 2]:
                            pe.wait_ge(load_done[k + 2], load_total[k + 2])
                        _, _, q, a, b = todo[places.index(i)]
                        transpose_group(k + 2, q, a, b)
                last.then_inc(chunk_used, 1)

            def output_block(c, slots, acc, m, operand):
                for half, (k0, k1) in enumerate(HALVES):
                    pe.wait_ge(rests, c + half + 1)
                    for k in range(k0, k1):
                        if operand is z and k == NB - 1:
                            pe.wait_ge(drained, 2 + NHI)
                        last = three(bank[acc][0:m, :], slots[half], k - k0, m, operand[:, k],
                                     k == 0, k == NB - 1, size(k))
                    last.then_inc(chunk_used, 1)

            groups_stored(NQ)
            with pe.Fori(0, (NHI - 1) // 2) as it:
                for odd in range(2):
                    pe.wait_ge(drained, odd + 1 + 2 * it)
                    output_block(chunk(odd, 0) + 4 * it, slots_of(odd), 6 + odd, P, g)
            pe.wait_ge(drained, NHI)
            output_block(chunk(NHI - 1, 0), slots_of(NHI - 1), 6 + (NHI - 1) % 2, TAIL, g)

            pe.wait_ge(drained, 2 + NHI - 1)
            with pe.Fori(0, (NB - 1) // 2) as it:
                for odd in range(2):
                    s0 = NHI + odd
                    pe.wait_ge(drained, s0 + 1 + 2 * it)
                    output_block(chunk(s0, 0) + 4 * it, slots_of(s0), 6 + s0 % 2, P, z)
            pe.wait_ge(drained, NSEQ)
            output_block(chunk(NSEQ - 1, 0), slots_of(NSEQ - 1), 6 + (NSEQ - 1) % 2, TAIL, z)


def kernel(x, adj):
    import numpy as np
    import concourse.bacc as bacc
    from concourse.bass_utils import run_bass_kernel_spmd

    nc = bacc.Bacc("TRN2", target_bir_lowering=False, num_devices=1)
    arrays, args = {}, []
    for name, a in (("x", x), ("adj", adj)):
        a = np.ascontiguousarray(a)
        arrays[f"in_{name}_dram"] = a
        args.append(nc.dram_tensor(f"in_{name}_dram", a.shape, mybir.dt.from_np(a.dtype), kind="ExternalInput").ap())
    shape = arrays["in_x_dram"].shape
    args.append(nc.dram_tensor("out_dram", shape, mybir.dt.float32, kind="ExternalOutput").ap())
    graph_layer(nc, *args)
    r = run_bass_kernel_spmd(nc, [arrays], core_ids=[0])
    return r.results[0]["out_dram"]
```

```python
import concourse.bass as bass
from concourse import mybir
from contextlib import ExitStack



CFG = (1, 1, 2, 3)


def graph_layer(nc: bass.Bass, x: bass.AP, A: bass.AP, out: bass.AP):
    f32 = mybir.dt.float32
    f32r = mybir.dt.float32r
    ALU = mybir.AluOpType
    ACT = mybir.ActivationFunctionType
    AX = mybir.AxisListType

    P = 128
    N, D = x.shape
    NB = -(-N // P)
    TAIL = N - (NB - 1) * P
    T64 = 64
    LO = 6
    HALVES = ((0, LO), (LO, NB))
    NHI = NB - LO
    NSEQ = NHI + NB
    SLOTS = 4
    EPS = 1e-5
    ACT_G, DVE_A, DVE_B, DVE_C = CFG
    TINY = 1.1754943508222875e-38

    def size(i):
        return TAIL if i == NB - 1 else P

    def end(i):
        return min(i * P, N)

    CUTS = ((0, 4), (4, 6), (6, 9), (9, NB))
    GROUPS = [[(max(a, n), b) for a, b in CUTS if b > n] for n in range(NB)]
    FIRST = [sum(len(g) for g in GROUPS[:n]) for n in range(NB + 1)]
    below = [max(a, n + 1) < b for n in range(NB) for a, b in GROUPS[n]]
    BELOW = [sum(below[:q]) for q in range(len(below) + 1)]
    LOW = [FIRST[n] + sum(b <= LO for a, b in GROUPS[n]) for n in range(NB)]
    PARTS = [1 + FIRST[n + 1] - LOW[n] + (n > LO) for n in range(NB)]
    EARLY = FIRST[2]
    PLACES = {4: (0, 5, 10, 15), 3: (0, 6, 12), 2: (0, 6), 1: (0,)}
    LATE = (10, 12, 14, 17)

    def chunk(s, half):
        return NB + 2 * s + half

    ctx = ExitStack()
    with ctx:
        def sb(name, shape, dt):
            return ctx.enter_context(nc.sbuf_tensor(name, shape, dt))

        def sem(name):
            return ctx.enter_context(nc.semaphore(name))

        def next_offset():
            return -(-nc.sbuf_base // 32) * 32

        def at(name, shape, dt, offset):
            return nc.alloc_sbuf_tensor_at(name, shape, dt, offset=offset)

        z_at = next_offset()
        sb("zone_z", [P, NB * 2 * D], f32)
        g_at = next_offset()
        sb("zone_g", [P, NB * 2 * D], f32)

        lo_bytes = NB * LO * P * 4
        A_lo = at("A_lo", [P, NB, LO * P], f32, z_at)
        x_in = at("x_in", [P, 3, D], f32, z_at + lo_bytes)
        xr = at("xr", [P, 2, D], f32, z_at + lo_bytes + 3 * D * 4)
        z = at("z", [P, NB, 2, D], f32r, z_at)
        g = at("g", [P, NB, 2, D], f32r, g_at)
        x_res = at("x_res", [P, NB, D], f32, g_at)
        y_out = at("y_out", [P, NB, D], f32, g_at + NB * D * 4)

        A_hi = sb("A_hi", [P, NB, N - LO * P], f32)
        AT = sb("AT", [P, NB, N], f32)
        ring = sb("ring", [P, SLOTS, 2, LO * P], f32r)
        ident = sb("ident", [P, P], f32)
        neg_half = sb("neg_half", [P, 2], f32)
        stats = sb("stats", [P, NB, 6], f32)
        moments = sb("moments", [P, NB, 2], f32)
        sums = sb("sums", [P, NB, 4], f32)
        degree = sb("degree", [P, NB], f32)
        positive = sb("positive", [P, NB], f32)
        base = sb("base", [P, NB, 2], f32)
        power = sb("power", [P, NB, 2], f32)
        g_scale = sb("g_scale", [P, NB], f32)
        z_scale = sb("z_scale", [P, NB], f32)

        bank = [ctx.enter_context(nc.psum_tensor(f"bank{b}", [P, D], f32)) for b in range(8)]

        load_lo = [sem(f"load_lo{n}") for n in range(LO)]
        load_hi = [sem(f"load_hi{n}") for n in range(NB - 1)]
        x_done = [sem(f"x_done{n}") for n in range(NB)]
        res_done = sem("res_done")
        out_done = sem("out_done")
        ident_zero = sem("ident_zero")
        ident_ready = sem("ident_ready")
        exponent_ready = sem("exponent_ready")
        transposed = sem("transposed")
        row_stored = sem("row_stored")
        at_stored = sem("at_stored")
        eye_added = sem("eye_added")
        c_added = sem("c_added")
        r_added = sem("r_added")
        heads = sem("heads")
        rests = sem("rests")
        chunk_used = sem("chunk_used")
        sums_ready = sem("sums_ready")
        stats_ready = sem("stats_ready")
        moments_ready = sem("moments_ready")
        var_ready = sem("var_ready")
        xr_ready = sem("xr_ready")
        degree_ready = sem("degree_ready")
        base_ready = sem("base_ready")
        power_ready = sem("power_ready")
        scale_ready = sem("scale_ready")
        g_head = sem("g_head")
        g_ready = sem("g_ready")
        z_scale_ready = sem("z_scale_ready")
        z_head = sem("z_head")
        drained = sem("drained")

        def S_blocks(rows, i0, i1):
            if i1 <= LO:
                return A_lo[:, rows, i0 * P:end(i1)]
            return A_hi[:, rows, i0 * P - LO * P:end(i1) - LO * P]

        def slots_of(s):
            return [chunk(s, half) % SLOTS for half in range(2)]

        def column(s):
            i = LO + s if s < NHI else s - NHI
            cols = size(i)
            if s < NHI:
                return (lambda ks, r: A_hi[0:r, ks, (i - LO) * P:(i - LO) * P + cols]), cols
            return (lambda ks, r: AT[0:r, ks, i * P:i * P + cols]), cols

        def group_banks(q):
            pair = 3 if q >= EARLY else (q + 3) % 4
            return bank[2 * pair], bank[2 * pair + 1]

        steps = [(n, j, FIRST[n] + j, a, b) for n in range(NB) for j, (a, b) in enumerate(GROUPS[n])]
        NQ = len(steps)

        def groups_of(n):
            return [s for s in steps if s[0] == n]

        full = (NB - 1) * P
        TAIL_PARTS = ((0, T64), (T64, TAIL))

        def row_block(n, i0, i1):
            return S_blocks(n, i0, i1), A[n * P:(n + 1) * P, i0 * P:end(i1)]

        def column_block(n, i0, i1):
            return (S_blocks(slice(i0, i1), n, n + 1),
                    A[i0 * P:i1 * P, n * P:(n + 1) * P].rearrange("(k p) c -> p k c", p=P))

        def tail_rows(i0, i1):
            return [(S_blocks(NB - 1, i0, i1)[p0:p1], A[full + p0:full + p1, i0 * P:end(i1)])
                    for p0, p1 in TAIL_PARTS]

        def loads_lo(n):
            found = [row_block(n, n, LO)]
            if n + 1 < LO:
                found.append(column_block(n, n + 1, LO))
            return found

        def loads_hi(n):
            found = [row_block(n, max(n, LO), NB)]
            if n + 1 < NB - 1:
                found.append(column_block(n, max(n + 1, LO), NB - 1))
            if n == 0:
                found += tail_rows(0, 1)
            if n == 1:
                found += tail_rows(1, LO) + tail_rows(LO, NB)
            return found

        block = ctx.enter_context(nc.Block())

        @block.sync
        def _(sp):
            for n in range(NB):
                if n < LO:
                    for dst, src in loads_lo(n):
                        sp.dma_start(dst, src).then_inc(load_lo[n], 16)
                if n >= 3:
                    sp.wait_ge(xr_ready, n - 2)
                for p0, p1 in ((0, P),) if n < NB - 1 else TAIL_PARTS:
                    sp.dma_start(x_in[p0:p1, n % 3, :], x[n * P + p0:n * P + p1, :]).then_inc(x_done[n], 16)
                if n < NB - 1:
                    for dst, src in loads_hi(n):
                        sp.dma_start(dst, src).then_inc(load_hi[n], 16)

            sp.wait_ge(chunk_used, chunk(NHI, 0))
            sp.dma_start(x_res[:, 0:NB - 1, :], x[0:full, :].rearrange("(k p) d -> p k d", p=P)
                         ).then_inc(res_done, 16)
            for p0, p1 in TAIL_PARTS:
                sp.dma_start(x_res[p0:p1, NB - 1, :], x[full + p0:full + p1, :]).then_inc(res_done, 16)
            with sp.Fori(0, NB - 1) as m:
                sp.wait_ge(drained, 2 + NHI + 1 + m)
                sp.dma_start(out[bass.ds(m * P, P), :], y_out[:, bass.ds(m, 1), :].rearrange("p o d -> p (o d)")
                             ).then_inc(out_done, 16)
            sp.wait_ge(drained, 2 + NSEQ)
            for p0, p1 in TAIL_PARTS:
                sp.dma_start(out[full + p0:full + p1, :], y_out[p0:p1, NB - 1, :]).then_inc(out_done, 16)
            sp.wait_ge(out_done, (NB + 1) * 16)

        @block.gpsimd
        def _(pool):
            nc.gpsimd.memset(ident[:], 0.0).then_inc(ident_zero, 1)
            nc.gpsimd.memset(neg_half[:], -0.5).then_inc(exponent_ready, 1)
            pool.wait_ge(ident_zero, 1)
            nc.gpsimd.affine_select(out=ident[:], in_=ident[:], compare_op=ALU.not_equal, fill=1.0, base=0,
                                    pattern=[[-1, P]], channel_multiplier=1).then_inc(ident_ready, 1)
            pool.wait_ge(exponent_ready, 1)

            def add_columns(n):
                for _, _, q, a, b in groups_of(n):
                    a = max(a, n + 1)
                    if a >= b:
                        continue
                    pool.wait_ge(at_stored, BELOW[q + 1])
                    parts = []
                    if b > a and min(b, NB - 1) > a:
                        parts.append((P, slice(a, min(b, NB - 1))))
                    if b == NB:
                        parts.append((TAIL, slice(NB - 1, NB)))
                    for r, ks in parts:
                        blocks = S_blocks(ks, n, n + 1)[0:r]
                        last = nc.gpsimd.tensor_tensor(blocks, blocks, AT[0:r, ks, n * P:(n + 1) * P], ALU.add)
                    last.then_inc(r_added, 1)

            def powers(n):
                r = size(n)
                pool.wait_ge(var_ready, n + 1)
                pool.wait_ge(base_ready, n + 1)
                nc.gpsimd.tensor_tensor(power[0:r, n, :], base[0:r, n, :], neg_half[0:r, :],
                                        ALU.pow).then_inc(power_ready, 1)

            add_columns(0)
            powers(0)
            add_columns(1)
            for n in range(1, NB):
                powers(n)
                if n + 1 < NB:
                    add_columns(n + 1)

        @block.scalar
        def _(act):
            def store_group(n, _, q, a, b):
                act.wait_ge(transposed, q + 1)
                row_bank, col_bank = group_banks(q)
                nc.scalar.copy(AT[0:size(n), n, a * P:end(b)],
                               row_bank[0:size(n), 0:end(b) - a * P]).then_inc(row_stored, 1)
                a2, full_end = max(a, n + 1), min(b, NB - 1)
                if a2 < b:
                    blocks = col_bank[:, :].rearrange("p (k c) -> p k c", c=P)
                    if full_end > a2:
                        last = nc.scalar.copy(AT[:, a2:full_end, n * P:(n + 1) * P],
                                              blocks[:, a2 - a:full_end - a, :])
                    if b == NB:
                        last = nc.scalar.copy(AT[0:TAIL, NB - 1, n * P:(n + 1) * P], blocks[0:TAIL, NB - 1 - a, :])
                    last.then_inc(at_stored, 1)

            def head_lo(n):
                r = size(n)
                act.wait_ge(c_added, LOW[n])
                if n > 0:
                    act.wait_ge(r_added, BELOW[FIRST[n]])
                if n >= SLOTS:
                    act.wait_ge(chunk_used, n - SLOTS + 1)
                nc.scalar.activation(ring[0:r, n % SLOTS, 0, :], A_lo[0:r, n, :], ACT.Copy,
                                     accum_out=sums[0:r, n, 0:1]).then_inc(heads, 1)

            def sum_below(n):
                r, w = size(n), (n - LO) * P
                nc.scalar.activation(A_hi[0:r, n, 0:w], A_hi[0:r, n, 0:w], ACT.Copy,
                                     accum_out=sums[0:r, n, PARTS[n] - 1:PARTS[n]]).then_inc(sums_ready, 1)

            def head_g(n):
                r = size(n)
                act.wait_ge(scale_ready, n + 1)
                nc.scalar.activation(g[0:r, n, 0, :], xr[0:r, n % 2, :], ACT.Copy,
                                     scale=g_scale[0:r, n:n + 1]).then_inc(g_head, 1)

            for group in groups_of(0):
                if group[3] == LO:
                    head_lo(0)
                store_group(*group)
            first, *others = groups_of(1)
            store_group(*first)
            head_g(0)
            for group in others:
                store_group(*group)
            for n in range(1, NB):
                head_lo(n)
                if n > LO:
                    sum_below(n)
                todo = groups_of(n + 1) if n + 1 < NB else []
                for group in todo[:ACT_G]:
                    store_group(*group)
                head_g(n)
                for group in todo[ACT_G:]:
                    store_group(*group)

            def head_column(c, slots, source, cols):
                for half, (k0, k1) in enumerate(HALVES):
                    act.wait_ge(chunk_used, c + half - SLOTS + 1)
                    v = ring[:, slots[half], 0, 0:(k1 - k0) * P].rearrange("p (k c) -> p k c", c=P)
                    kf = min(k1, NB - 1)
                    last = nc.scalar.copy(v[:, 0:kf - k0, 0:cols], source(slice(k0, kf), P))
                    if k1 == NB:
                        last = nc.scalar.copy(v[0:TAIL, kf - k0, 0:cols], source(kf, TAIL))
                    last.then_inc(heads, 1)

            def head_of(s):
                head_column(chunk(s, 0), slots_of(s), *column(s))

            act.wait_ge(sums_ready, NB - 1 - LO)
            for s in (0, 1):
                head_of(s)

            def z_evac(i, src):
                r = size(i)
                nc.scalar.activation(z[0:r, i, 0, :], src[0:r, :], ACT.Copy,
                                     scale=z_scale[0:r, i:i + 1]).then_inc(z_head, 1)

            act.wait_ge(chunk_used, NB)
            act.wait_ge(rests, NB)
            act.wait_ge(g_ready, NB)
            act.wait_ge(z_scale_ready, 1)
            for i in range(LO):
                z_evac(i, bank[i])
            for s in range(2, 2 + NHI):
                head_of(s)
                act.wait_ge(chunk_used, chunk(s - 2, 2))
                z_evac(LO + s - 2, bank[6 + (s - 2) % 2])
            with act.Fori(0, (NSEQ - 1 - (2 + NHI)) // 2) as it:
                for odd in range(2):
                    s0 = 2 + NHI + odd
                    head_column(chunk(s0, 0) + 4 * it, slots_of(s0),
                                lambda ks, r: AT[0:r, ks, bass.ds((s0 - NHI + 2 * it) * P, P)], P)
            head_of(NSEQ - 1)

        @block.vector
        def _(dve):
            def statistics(n):
                r = size(n)
                dve.wait_ge(x_done[n], 16 if n < NB - 1 else 32)
                nc.vector.bn_stats(stats[0:r, n, :], x_in[0:r, n % 3, :]).then_inc(stats_ready, 1)

            def mean_and_variance(n):
                r = size(n)
                dve.wait_ge(stats_ready, n + 1)
                nc.vector.bn_aggr(moments[0:r, n, :], stats[0:r, n, :]).then_inc(moments_ready, 1)

            def centre(n):
                r = size(n)
                dve.wait_ge(moments_ready, n + 1)
                nc.vector.tensor_scalar(base[0:r, n, 0:1], moments[0:r, n, 1:2], EPS, None,
                                        ALU.add).then_inc(var_ready, 1)
                nc.vector.tensor_scalar(xr[0:r, n % 2, :], x_in[0:r, n % 3, :], moments[0:r, n, 0:1], 0.0,
                                        ALU.subtract, ALU.max).then_inc(xr_ready, 1)

            def add_group(n, _, q, a, b):
                r = size(n)
                dve.wait_ge(row_stored, q + 1)
                if a == n:
                    diag = S_blocks(n, n, n + 1)[0:r]
                    nc.vector.scalar_tensor_tensor(out=diag, in0=ident[0:r, 0:r], scalar=2.0, in1=diag,
                                                   op0=ALU.mult, op1=ALU.add).then_inc(eye_added, 1)
                    dve.wait_ge(eye_added, n + 1)
                blocks = S_blocks(n, a, b)[0:r]
                if b <= LO:
                    last = nc.vector.tensor_tensor(blocks, blocks, AT[0:r, n, a * P:end(b)], ALU.add)
                else:
                    part = 1 + q - LOW[n]
                    last = nc.vector.scalar_tensor_tensor(out=blocks, in0=blocks, scalar=1.0,
                                                          in1=AT[0:r, n, a * P:end(b)], op0=ALU.mult, op1=ALU.add,
                                                          accum_out=sums[0:r, n, part:part + 1])
                last.then_inc(c_added, 1)

            def degrees(n):
                r = size(n)
                dve.wait_ge(heads, n + 1)
                dve.wait_ge(c_added, FIRST[n + 1])
                if n > LO:
                    dve.wait_ge(sums_ready, n - LO)
                nc.vector.reduce_sum(degree[0:r, n:n + 1], sums[0:r, n, 0:PARTS[n]], AX.X).then_inc(degree_ready, 1)
                dve.wait_ge(degree_ready, n + 1)
                nc.vector.tensor_scalar(positive[0:r, n:n + 1], degree[0:r, n:n + 1], 0.0, None, ALU.is_gt)
                nc.vector.tensor_scalar(base[0:r, n, 1:2], degree[0:r, n:n + 1], 0.5, TINY,
                                        ALU.mult, ALU.max).then_inc(base_ready, 1)

            def rest_lo(n):
                r = size(n)
                dve.wait_ge(heads, n + 1)
                nc.vector.tensor_tensor(ring[0:r, n % SLOTS, 1, :], A_lo[0:r, n, :],
                                        ring[0:r, n % SLOTS, 0, :].bitcast(f32), ALU.subtract).then_inc(rests, 1)

            def scale_g(n):
                r = size(n)
                dve.wait_ge(power_ready, n + 1)
                dve.wait_ge(base_ready, n + 1)
                nc.vector.tensor_scalar(g_scale[0:r, n:n + 1], power[0:r, n, 1:2], positive[0:r, n:n + 1],
                                        power[0:r, n, 0:1], ALU.mult, ALU.mult).then_inc(scale_ready, 1)

            def rest_g(n):
                r = size(n)
                dve.wait_ge(g_head, n + 1)
                nc.vector.scalar_tensor_tensor(out=g[0:r, n, 1, :], in0=xr[0:r, n % 2, :],
                                               scalar=g_scale[0:r, n:n + 1], in1=g[0:r, n, 0, :].bitcast(f32),
                                               op0=ALU.mult, op1=ALU.subtract).then_inc(g_ready, 1)

            dve.wait_ge(ident_ready, 1)
            todo = groups_of(0)
            for group in todo[:2]:
                add_group(*group)
            statistics(0)
            mean_and_variance(0)
            centre(0)
            for group in todo[2:]:
                add_group(*group)
            degrees(0)
            rest_lo(0)
            scale_g(0)
            rest_g(0)
            todo = groups_of(1)
            for group in todo:
                add_group(*group)
            statistics(1)
            mean_and_variance(1)
            centre(1)
            for n in range(1, NB):
                degrees(n)
                rest_lo(n)
                scale_g(n)
                todo = groups_of(n + 1) if n + 1 < NB else []
                for group in todo[:DVE_A]:
                    add_group(*group)
                rest_g(n)
                if n + 1 < NB:
                    for group in todo[DVE_A:DVE_B]:
                        add_group(*group)
                    statistics(n + 1)
                    for group in todo[DVE_B:DVE_C]:
                        add_group(*group)
                    mean_and_variance(n + 1)
                    for group in todo[DVE_C:]:
                        add_group(*group)
                    centre(n + 1)

            nc.vector.scalar_tensor_tensor(out=z_scale[:, 0:NB - 1], in0=power[:, 0:NB - 1, 1], scalar=0.5,
                                           in1=positive[:, 0:NB - 1], op0=ALU.mult, op1=ALU.mult)
            nc.vector.scalar_tensor_tensor(out=z_scale[0:TAIL, NB - 1:], in0=power[0:TAIL, NB - 1:, 1], scalar=0.5,
                                           in1=positive[0:TAIL, NB - 1:], op0=ALU.mult,
                                           op1=ALU.mult).then_inc(z_scale_ready, 1)
            dve.sem_inc(drained, 2)

            def rest_column(c, slots, source, cols):
                for half, (k0, k1) in enumerate(HALVES):
                    dve.wait_ge(heads, c + half + 1)
                    v = ring[:, slots[half], :, 0:(k1 - k0) * P].rearrange("p t (k c) -> p t k c", c=P)
                    kf = min(k1, NB - 1)
                    last = nc.vector.tensor_tensor(v[:, 1, 0:kf - k0, 0:cols], source(slice(k0, kf), P),
                                                   v[:, 0, 0:kf - k0, 0:cols].bitcast(f32), ALU.subtract)
                    if k1 == NB:
                        last = nc.vector.tensor_tensor(v[0:TAIL, 1, kf - k0, 0:cols], source(kf, TAIL),
                                                       v[0:TAIL, 0, kf - k0, 0:cols].bitcast(f32), ALU.subtract)
                    last.then_inc(rests, 1)

            def rest_of(s):
                rest_column(chunk(s, 0), slots_of(s), *column(s))

            def z_rest(i, src):
                r = size(i)
                dve.wait_ge(z_head, i + 1)
                last = nc.vector.scalar_tensor_tensor(out=z[0:r, i, 1, :], in0=src[0:r, :],
                                                      scalar=z_scale[0:r, i:i + 1],
                                                      in1=z[0:r, i, 0, :].bitcast(f32),
                                                      op0=ALU.mult, op1=ALU.subtract)
                return last

            for s in (0, 1):
                rest_of(s)
            for i in range(LO):
                z_rest(i, bank[i])
            for s in range(2, 2 + NHI):
                rest_of(s)
                z_rest(LO + s - 2, bank[6 + (s - 2) % 2]).then_inc(drained, 1)
            dve.wait_ge(res_done, 48)

            def result(m, slot, r=P):
                dst = y_out[0:r, bass.ds(m, 1), :].rearrange("p o d -> p (o d)")
                res = x_res[0:r, bass.ds(m, 1), :].rearrange("p o d -> p (o d)")
                nc.vector.tensor_tensor(dst, bank[slot][0:r, :], res,
                                        ALU.add).then_inc(drained, 1)

            with dve.Fori(0, (NSEQ - 1 - (2 + NHI)) // 2) as it:
                for odd in range(2):
                    s0 = 2 + NHI + odd
                    rest_column(chunk(s0, 0) + 4 * it, slots_of(s0),
                                lambda ks, r: AT[0:r, ks, bass.ds((s0 - NHI + 2 * it) * P, P)], P)
                    dve.wait_ge(chunk_used, chunk(s0 - 2, 2) + 4 * it)
                    result(odd + 2 * it, 6 + (s0 - 2) % 2)
            rest_of(NSEQ - 1)
            for s in range(NSEQ - 3, NSEQ):
                dve.wait_ge(chunk_used, chunk(s, 2))
                result(s - NHI, 6 + s % 2, size(s - NHI))

        @block.tensor
        def _(pe):
            def groups_stored(q):
                pe.wait_ge(row_stored, q)
                pe.wait_ge(at_stored, BELOW[q])

            def transpose_group(n, _, q, a, b):
                if q < EARLY:
                    if q >= 4:
                        groups_stored(q - 3)
                else:
                    groups_stored(q)
                if b <= LO:
                    pe.wait_ge(load_lo[n], 16 * len(loads_lo(n)))
                elif n < NB - 1:
                    pe.wait_ge(load_hi[n], 16 * len(loads_hi(n)))
                row_bank, col_bank = group_banks(q)
                r = size(n)
                for i in range(a, b):
                    o = (i - a) * P
                    last = nc.tensor.transpose(row_bank[0:r, o:o + size(i)], S_blocks(i, n, n + 1)[0:size(i)],
                                               ident[0:size(i), 0:size(i)])
                    if i > n:
                        last = nc.tensor.transpose(col_bank[0:size(i), o:o + r], S_blocks(n, i, i + 1)[0:r],
                                                   ident[0:r, 0:r])
                last.then_inc(transposed, 1)

            def product(dst, slot, b, m, rhs, r, parts, first, final):
                stationary = ring[0:r, slot, parts[0], b * P:b * P + m]
                return nc.tensor.matmul(dst, stationary, rhs[0:r, parts[1], :], start=first, stop=final)

            pe.wait_ge(ident_ready, 1)
            for n in (0, 1):
                for group in groups_of(n):
                    transpose_group(*group)

            groups_stored(EARLY)
            for k in range(NB):
                todo = dict(zip(LATE if k == 0 else PLACES[len(groups_of(k + 2))], groups_of(k + 2))
                            ) if k + 2 < NB else {}
                if k == 0:
                    order = [(i, *parts) for parts in ((0, 0), (1, 0), (0, 1)) for i in range(LO)]
                    pe.wait_ge(heads, 1)
                    pe.wait_ge(g_head, 1)
                else:
                    order = [(i, *parts) for i in range(LO) for parts in ((0, 0), (0, 1), (1, 0))]
                    pe.wait_ge(rests, k + 1)
                    pe.wait_ge(g_ready, k + 1)
                seen = [0] * LO
                for at_product, (i, part, g_part) in enumerate(order):
                    if k == 0 and at_product == LO:
                        pe.wait_ge(rests, 1)
                    if k == 0 and at_product == 2 * LO:
                        pe.wait_ge(g_ready, 1)
                    last = product(bank[i][:, :], k % SLOTS, i, P, g[:, k], size(k), (part, g_part),
                                   k == 0 and seen[i] == 0, k == NB - 1 and seen[i] == 2)
                    seen[i] += 1
                    if at_product == len(order) - 1:
                        last.then_inc(chunk_used, 1)
                    if at_product in todo:
                        transpose_group(*todo[at_product])

            def output_block(c, slots, acc, m, operand):
                for half, (k0, k1) in enumerate(HALVES):
                    pe.wait_ge(rests, c + half + 1)
                    for k in range(k0, k1):
                        if operand is z and k == NB - 1:
                            pe.wait_ge(drained, 2 + NHI)
                        for t, parts in enumerate(((0, 0), (0, 1), (1, 0))):
                            last = product(bank[acc][0:m, :], slots[half], k - k0, m, operand[:, k], size(k),
                                           parts, k == 0 and t == 0, k == NB - 1 and t == 2)
                    last.then_inc(chunk_used, 1)

            groups_stored(NQ)
            with pe.Fori(0, (NHI - 1) // 2) as it:
                for odd in range(2):
                    pe.wait_ge(drained, odd + 1 + 2 * it)
                    output_block(chunk(odd, 0) + 4 * it, slots_of(odd), 6 + odd, P, g)
            pe.wait_ge(drained, NHI)
            output_block(chunk(NHI - 1, 0), slots_of(NHI - 1), 6 + (NHI - 1) % 2, TAIL, g)

            pe.wait_ge(drained, 2 + NHI - 1)
            with pe.Fori(0, (NB - 1) // 2) as it:
                for odd in range(2):
                    s0 = NHI + odd
                    pe.wait_ge(drained, s0 + 1 + 2 * it)
                    output_block(chunk(s0, 0) + 4 * it, slots_of(s0), 6 + s0 % 2, P, z)
            pe.wait_ge(drained, NSEQ)
            output_block(chunk(NSEQ - 1, 0), slots_of(NSEQ - 1), 6 + (NSEQ - 1) % 2, TAIL, z)


def kernel(x, adj):
    import numpy as np
    import concourse.bacc as bacc
    from concourse.bass_utils import run_bass_kernel_spmd

    nc = bacc.Bacc("TRN2", target_bir_lowering=False, num_devices=1)
    arrays, args = {}, []
    for name, a in (("x", x), ("adj", adj)):
        a = np.ascontiguousarray(a)
        arrays[f"in_{name}_dram"] = a
        args.append(nc.dram_tensor(f"in_{name}_dram", a.shape, mybir.dt.from_np(a.dtype), kind="ExternalInput").ap())
    shape = arrays["in_x_dram"].shape
    args.append(nc.dram_tensor("out_dram", shape, mybir.dt.float32, kind="ExternalOutput").ap())
    graph_layer(nc, *args)
    r = run_bass_kernel_spmd(nc, [arrays], core_ids=[0])
    return r.results[0]["out_dram"]
```

```python
import concourse.bass as bass
from concourse import mybir
from contextlib import ExitStack



def graph_layer(nc: bass.Bass, x: bass.AP, A: bass.AP, out: bass.AP):
    f32 = mybir.dt.float32
    f32r = mybir.dt.float32r
    ALU = mybir.AluOpType
    ACT = mybir.ActivationFunctionType
    AX = mybir.AxisListType

    P = 128
    N, D = x.shape
    NB = -(-N // P)
    TAIL = N - (NB - 1) * P
    T64 = 64
    LO = 6
    HALVES = ((0, LO), (LO, NB))
    NHI = NB - LO
    NSEQ = NHI + NB
    SLOTS = 4
    EPS = 1e-5
    TINY = 1.1754943508222875e-38

    SECOND = [*range(LO, NB - 2), NB - 1, NB - 2]
    TAIL_AT = SECOND.index(NB - 1)

    def size(i):
        return TAIL if i == NB - 1 else P

    def end(i):
        return min(i * P, N)

    CUTS = ((0, 4), (4, 6), (6, 9), (9, NB))
    GROUPS = [[(max(a, n), b) for a, b in CUTS if b > n] for n in range(NB)]
    FIRST = [sum(len(g) for g in GROUPS[:n]) for n in range(NB + 1)]
    below = [max(a, n + 1) < b for n in range(NB) for a, b in GROUPS[n]]
    BELOW = [sum(below[:q]) for q in range(len(below) + 1)]
    LOW = [FIRST[n] + sum(b <= LO for a, b in GROUPS[n]) for n in range(NB)]
    PARTS = [len(GROUPS[0])] + [1 + FIRST[n + 1] - LOW[n] + (n > LO) for n in range(1, NB)]
    EARLY = FIRST[2]
    PLACES = {4: (2, 7, 12, 17), 3: (2, 8, 14), 2: (0, 6), 1: (0,)}
    LATE = (8, 11, 14, 17)
    BEFORE_G = [0, 2, 2] + [1] * (NB - 3)
    X_AFTER = (0, 1, 2, 4, 5)
    MANY = 4
    SUM_STEP = 8

    DUP = P - TAIL
    MIX = 3 * TAIL - P
    X, Y = NB - 1, NB

    def chunk(s, half):
        return NB - 1 if s == half == 0 else NB + 2 * s + half

    def step_chunk(k):
        return k if k < NB - 1 else NB

    ctx = ExitStack()
    with ctx:
        def sb(name, shape, dt):
            return ctx.enter_context(nc.sbuf_tensor(name, shape, dt))

        def sem(name):
            return ctx.enter_context(nc.semaphore(name))

        def next_offset():
            return -(-nc.sbuf_base // 32) * 32

        def at(name, shape, dt, offset):
            return nc.alloc_sbuf_tensor_at(name, shape, dt, offset=offset)

        z_at = next_offset()
        sb("zone_z", [P, NB * 2 * D], f32)
        g_at = next_offset()
        sb("zone_g", [P, NB * 2 * D], f32)

        lo_bytes = (NB + 1) * LO * P * 4
        A_lo = at("A_lo", [P, NB + 1, LO * P], f32, z_at)
        x_in = at("x_in", [P, 2, D], f32, z_at + lo_bytes)
        xr = at("xr", [P, 2, D], f32, z_at + lo_bytes + 2 * D * 4)
        z = at("z", [P, NB, 2, D], f32r, z_at)
        g = at("g", [P, NB, 2, D], f32r, g_at)
        x_res = at("x_res", [P, NB, D], f32, g_at)
        y_out = at("y_out", [P, NB, D], f32, g_at + NB * D * 4)

        A_hi = sb("A_hi", [P, NB + 1, N - LO * P], f32)
        AT = sb("AT", [P, NB + 1, N], f32)
        ring = sb("ring", [P, SLOTS, 2, LO * P], f32r)
        rest_tail = sb("rest_tail", [P, D], f32r)
        minus_rests = sb("minus_rests", [P, 1], f32)
        ident = sb("ident", [P, P], f32)
        neg_half = sb("neg_half", [P, 2], f32)
        stats = sb("stats", [P, NB, 6], f32)
        moments = sb("moments", [P, NB, 2], f32)
        sums = sb("sums", [P, NB, 4], f32)
        degree = sb("degree", [P, NB], f32)
        positive = sb("positive", [P, NB], f32)
        base = sb("base", [P, NB, 2], f32)
        power = sb("power", [P, NB, 2], f32)
        g_scale = sb("g_scale", [P, NB], f32)
        z_scale = sb("z_scale", [P, NB], f32)

        bank = [ctx.enter_context(nc.psum_tensor(f"bank{b}", [P, D], f32)) for b in range(8)]

        load_lo = [sem(f"load_lo{n}") for n in range(LO)]
        load_hi = [sem(f"load_hi{n}") for n in range(NB - 1)]
        first_lo = sem("first_lo")
        first_hi = sem("first_hi")
        x_done = [sem(f"x_done{n}") for n in range(NB)]
        res_done = sem("res_done")
        tail_lo_done = sem("tail_lo_done")
        tail_hi_done = sem("tail_hi_done")
        tail_at_done = sem("tail_at_done")
        tail_g_done = sem("tail_g_done")
        tail_z_done = sem("tail_z_done")
        out_done = sem("out_done")
        minus_ones = sem("minus_ones")
        minus_ready = sem("minus_ready")
        ident_zero = sem("ident_zero")
        ident_ready = sem("ident_ready")
        exponent_ready = sem("exponent_ready")
        row_transposed = sem("row_transposed")
        col_transposed = sem("col_transposed")
        row_stored = sem("row_stored")
        col_stored = sem("col_stored")
        eye_added = sem("eye_added")
        row_added = sem("row_added")
        col_added = sem("col_added")
        heads = sem("heads")
        rests = sem("rests")
        chunk_used = sem("chunk_used")
        sums_ready = sem("sums_ready")
        stats_ready = sem("stats_ready")
        moments_ready = sem("moments_ready")
        var_ready = sem("var_ready")
        xr_ready = sem("xr_ready")
        degree_ready = sem("degree_ready")
        base_ready = sem("base_ready")
        power_ready = sem("power_ready")
        scale_ready = sem("scale_ready")
        g_head = sem("g_head")
        g_ready = sem("g_ready")
        z_scale_ready = sem("z_scale_ready")
        z_head = sem("z_head")
        drained = sem("drained")

        def S_blocks(rows, i0, i1):
            if i1 <= LO:
                return A_lo[:, rows, i0 * P:end(i1)]
            return A_hi[:, rows, i0 * P - LO * P:end(i1) - LO * P]

        def slots_of(s):
            return [chunk(s, half) % SLOTS for half in range(2)]

        def column(s):
            i = SECOND[s] if s < NHI else s - NHI
            cols = size(i)
            if s < NHI:
                return (lambda ks, r: A_hi[0:r, ks, (i - LO) * P:(i - LO) * P + cols]), cols
            return (lambda ks, r: AT[0:r, ks, i * P:i * P + cols]), cols

        LAST_IN = [max(q for q in range(EARLY) if (q + 3) % 4 == pair) for pair in range(LO // 2)]

        def group_banks(q):
            pair = 3 if q >= EARLY else (q + 3) % 4
            return bank[2 * pair], bank[2 * pair + 1]

        steps = [(n, j, FIRST[n] + j, a, b) for n in range(NB) for j, (a, b) in enumerate(GROUPS[n])]
        NQ = len(steps)

        def groups_of(n):
            return [s for s in steps if s[0] == n]

        full = (NB - 1) * P
        TAIL_PARTS = ((0, T64), (T64, TAIL))

        def row_block(n, i0, i1):
            return S_blocks(n, i0, i1), A[n * P:(n + 1) * P, i0 * P:end(i1)]

        def column_block(n, i0, i1):
            return (S_blocks(slice(i0, i1), n, n + 1),
                    A[i0 * P:i1 * P, n * P:(n + 1) * P].rearrange("(k p) c -> p k c", p=P))

        def tail_rows(i0, i1):
            return [(S_blocks(NB - 1, i0, i1)[p0:p1], A[full + p0:full + p1, i0 * P:end(i1)])
                    for p0, p1 in TAIL_PARTS]

        def loads_lo(n):
            found = [row_block(n, n, LO)] if n > 0 else []
            if n + 1 < LO:
                found.append(column_block(n, n + 1, LO))
            return found

        def loads_hi(n):
            found = [row_block(n, max(n, LO), NB)] if n > 0 else []
            if n + 1 < NB - 1:
                found.append(column_block(n, max(n + 1, LO), NB - 1))
            if n == 0:
                found += tail_rows(0, 2)
            if n == 2:
                found += tail_rows(2, LO) + tail_rows(LO, NB)
            return found

        block = ctx.enter_context(nc.Block())

        @block.sync
        def _(sp):
            def load_x(m):
                if m >= 2:
                    sp.wait_ge(xr_ready, m - 1)
                for p0, p1 in ((0, P),) if m < NB - 1 else TAIL_PARTS:
                    sp.dma_start(x_in[p0:p1, m % 2, :], x[m * P + p0:m * P + p1, :]).then_inc(x_done[m], 16)

            for n in range(NB - 1):
                if n == 0:
                    sp.dma_start(*row_block(0, 0, LO)).then_inc(first_lo, 16)
                if n < LO:
                    for dst, src in loads_lo(n):
                        sp.dma_start(dst, src).then_inc(load_lo[n], 16)
                if n == 0:
                    sp.dma_start(*row_block(0, LO, NB)).then_inc(first_hi, 16)
                for dst, src in loads_hi(n):
                    sp.dma_start(dst, src).then_inc(load_hi[n], 16)
                if n in X_AFTER:
                    load_x(X_AFTER.index(n))
            for m in range(len(X_AFTER), LO + 1):
                load_x(m)

            def repeat_tail(t, done):
                for dst, block, src in ((slice(TAIL, P), X, slice(0, DUP)), (slice(0, T64), Y, slice(0, T64)),
                                        (slice(T64, TAIL), Y, slice(T64, TAIL)),
                                        (slice(TAIL, MIX), Y, slice(DUP, TAIL))):
                    sp.dma_start(t[dst, block, :], t[src, X, :]).then_inc(done, 16)

            sp.wait_ge(col_added, BELOW[FIRST[LO]])
            repeat_tail(A_lo, tail_lo_done)
            for m in range(LO + 1, NB):
                load_x(m)
            sp.wait_ge(row_added, NQ)
            sp.wait_ge(col_added, BELOW[NQ])
            sp.wait_ge(sums_ready, NB - LO)
            repeat_tail(A_hi, tail_hi_done)
            sp.wait_ge(g_ready, NB)
            sp.dma_start(g[TAIL:P, NB - 1, 0, :].bitcast(f32),
                         rest_tail[0:DUP, :].bitcast(f32)).then_inc(tail_g_done, 16)
            sp.dma_start(g[TAIL:MIX, NB - 1, 1, :].bitcast(f32),
                         rest_tail[DUP:TAIL, :].bitcast(f32)).then_inc(tail_g_done, 16)
            sp.wait_ge(row_stored, NQ)
            sp.wait_ge(col_stored, BELOW[NQ])
            repeat_tail(AT, tail_at_done)

            sp.wait_ge(drained, TAIL_AT + 1)
            sp.dma_start(z[TAIL:P, NB - 1, 0, :].bitcast(f32),
                         rest_tail[0:DUP, :].bitcast(f32)).then_inc(tail_z_done, 16)
            sp.dma_start(z[TAIL:MIX, NB - 1, 1, :].bitcast(f32),
                         rest_tail[DUP:TAIL, :].bitcast(f32)).then_inc(tail_z_done, 16)
            sp.wait_ge(chunk_used, chunk(NHI, 0))
            sp.dma_start(x_res[:, 0:NB - 1, :], x[0:full, :].rearrange("(k p) d -> p k d", p=P)
                         ).then_inc(res_done, 16)
            for p0, p1 in TAIL_PARTS:
                sp.dma_start(x_res[p0:p1, NB - 1, :], x[full + p0:full + p1, :]).then_inc(res_done, 16)
            with sp.Fori(0, NB - 1) as m:
                sp.wait_ge(drained, NHI + 1 + m)
                sp.dma_start(out[bass.ds(m * P, P), :], y_out[:, bass.ds(m, 1), :].rearrange("p o d -> p (o d)")
                             ).then_inc(out_done, 16)
            sp.wait_ge(drained, NSEQ)
            for p0, p1 in TAIL_PARTS:
                sp.dma_start(out[full + p0:full + p1, :], y_out[p0:p1, NB - 1, :]).then_inc(out_done, 16)
            sp.wait_ge(out_done, (NB + 1) * 16)

        @block.gpsimd
        def _(pool):
            nc.gpsimd.memset(ident[:], 0.0).then_inc(ident_zero, 1)
            nc.gpsimd.memset(neg_half[:], -0.5).then_inc(exponent_ready, 1)
            pool.wait_ge(ident_zero, 1)
            nc.gpsimd.affine_select(out=ident[:], in_=ident[:], compare_op=ALU.not_equal, fill=1.0, base=0,
                                    pattern=[[-1, P]], channel_multiplier=1).then_inc(ident_ready, 1)
            nc.gpsimd.memset(minus_rests[:], -1.0).then_inc(minus_ones, 1)
            pool.wait_ge(minus_ones, 1)
            nc.gpsimd.affine_select(out=minus_rests[:], in_=minus_rests[:], compare_op=ALU.is_gt, fill=0.0,
                                    base=TAIL, pattern=[[0, 1]], channel_multiplier=-1).then_inc(minus_ready, 1)
            pool.wait_ge(exponent_ready, 1)

            def add_columns(n, groups):
                for _, _, q, a, b in groups:
                    a = max(a, n + 1)
                    if a >= b:
                        continue
                    pool.wait_ge(col_stored, BELOW[q + 1])
                    pool.wait_ge(row_transposed, q + 1)
                    parts = []
                    if b > a and min(b, NB - 1) > a:
                        parts.append((P, slice(a, min(b, NB - 1))))
                    if b == NB:
                        parts.append((TAIL, slice(NB - 1, NB)))
                    for r, ks in parts:
                        blocks = S_blocks(ks, n, n + 1)[0:r]
                        last = nc.gpsimd.tensor_tensor(blocks, blocks, AT[0:r, ks, n * P:(n + 1) * P], ALU.add)
                    last.then_inc(col_added, 1)

            def powers(n):
                r = size(n)
                pool.wait_ge(var_ready, n + 1)
                pool.wait_ge(base_ready, n + 1)
                nc.gpsimd.tensor_tensor(power[0:r, n, :], base[0:r, n, :], neg_half[0:r, :],
                                        ALU.pow).then_inc(power_ready, 1)

            add_columns(0, groups_of(0)[:2])
            powers(0)
            add_columns(0, groups_of(0)[2:])
            add_columns(1, groups_of(1))
            for n in range(1, NB):
                powers(n)
                if n + 1 < NB:
                    add_columns(n + 1, groups_of(n + 1))

        @block.scalar
        def _(act):
            def store_row(n, _, q, a, b):
                act.wait_ge(row_transposed, q + 1)
                nc.scalar.copy(AT[0:size(n), n, a * P:end(b)],
                               group_banks(q)[0][0:size(n), 0:end(b) - a * P]).then_inc(row_stored, 1)

            def store_column(n, _, q, a, b):
                a2, full_end = max(a, n + 1), min(b, NB - 1)
                if a2 >= b:
                    return
                act.wait_ge(col_transposed, BELOW[q + 1])
                blocks = group_banks(q)[1][:, :].rearrange("p (k c) -> p k c", c=P)
                if full_end > a2:
                    last = nc.scalar.copy(AT[:, a2:full_end, n * P:(n + 1) * P],
                                          blocks[:, a2 - a:full_end - a, :])
                if b == NB:
                    last = nc.scalar.copy(AT[0:TAIL, NB - 1, n * P:(n + 1) * P], blocks[0:TAIL, NB - 1 - a, :])
                last.then_inc(col_stored, 1)

            def store_group(*group):
                store_row(*group)
                store_column(*group)

            def head_lo(n):
                r, c = P, step_chunk(n)
                act.wait_ge(row_added, LOW[n])
                if n > 0:
                    act.wait_ge(col_added, BELOW[FIRST[n]])
                if n == NB - 1:
                    act.wait_ge(tail_lo_done, 64)
                if c >= SLOTS:
                    act.wait_ge(chunk_used, c - SLOTS + 1)
                nc.scalar.activation(ring[0:r, c % SLOTS, 0, :], A_lo[0:r, n, :], ACT.Copy,
                                     accum_out=sums[0:r, n, 0:1] if 0 < n < NB - 1 else None).then_inc(heads, 1)

            def sum_below(n):
                r, w = size(n), (n - LO) * P
                act.wait_ge(col_added, BELOW[FIRST[n]])
                nc.scalar.activation(A_hi[0:r, n, 0:w], A_hi[0:r, n, 0:w], ACT.Copy,
                                     accum_out=sums[0:r, n, PARTS[n] - 1:PARTS[n]]).then_inc(sums_ready, 1)

            def tail_sum_lo():
                act.wait_ge(tail_lo_done, 64)
                nc.scalar.activation(A_lo[0:TAIL, X, :], A_lo[0:TAIL, X, :], ACT.Copy,
                                     accum_out=sums[0:TAIL, X, 0:1]).then_inc(sums_ready, 1)

            def head_g(n):
                r = size(n)
                act.wait_ge(scale_ready, n + 1)
                for part in (0,) if n < NB - 1 else (0, 1):
                    nc.scalar.activation(g[0:r, n, part, :], xr[0:r, n % 2, :], ACT.Copy,
                                         scale=g_scale[0:r, n:n + 1]).then_inc(g_head, 1)

            def head_half(c, slot, half, source, cols):
                k0, k1 = HALVES[half]
                act.wait_ge(chunk_used, c - SLOTS + 1)
                v = ring[:, slot, 0, 0:(k1 - k0) * P].rearrange("p (k c) -> p k c", c=P)
                nc.scalar.copy(v[:, :, 0:cols], source(slice(k0, k1), P)).then_inc(heads, 1)

            def head_of(s, halves=(0, 1)):
                for half in halves:
                    head_half(chunk(s, half), slots_of(s)[half], half, *column(s))

            for two in (groups_of(0)[:2], groups_of(0)[2:]):
                for group in two:
                    store_column(*group)
                for group in two:
                    store_row(*group)
            head_lo(0)
            for group in groups_of(1)[:2]:
                store_group(*group)
            head_g(0)
            for group in groups_of(1)[2:]:
                store_group(*group)
            for n in range(1, NB):
                if n == NB - 1:
                    sum_below(n)
                    head_of(0, (0,))
                head_lo(n)
                if LO < n < NB - 1:
                    sum_below(n)
                if n == SUM_STEP:
                    tail_sum_lo()
                todo = groups_of(n + 1) if n + 1 < NB else []
                for group in todo[:BEFORE_G[n]]:
                    store_group(*group)
                head_g(n)
                for group in todo[BEFORE_G[n]:]:
                    store_group(*group)

            act.wait_ge(sums_ready, NB - LO)
            act.wait_ge(tail_hi_done, 64)
            head_of(0, (1,))
            head_of(1)

            def z_evac(i, src):
                r = size(i)
                for part in (0,) if i < NB - 1 else (0, 1):
                    nc.scalar.activation(z[0:r, i, part, :], src[0:r, :], ACT.Copy,
                                         scale=z_scale[0:r, i:i + 1]).then_inc(z_head, 1)

            act.wait_ge(chunk_used, NB + 1)
            act.wait_ge(rests, NB + 1)
            act.wait_ge(g_ready, NB)
            act.wait_ge(z_scale_ready, 1)
            for i in range(LO):
                z_evac(i, bank[i])
            for s in range(2, 2 + NHI):
                if s == NHI:
                    act.wait_ge(tail_at_done, 64)
                head_of(s)
                act.wait_ge(chunk_used, chunk(s - 2, 2))
                z_evac(SECOND[s - 2], bank[6 + (s - 2) % 2])
            with act.Fori(0, (NSEQ - 1 - (2 + NHI)) // 2) as it:
                for odd in range(2):
                    s0 = 2 + NHI + odd
                    for half in range(2):
                        head_half(chunk(s0, half) + 4 * it, slots_of(s0)[half], half,
                                  lambda ks, r: AT[0:r, ks, bass.ds((s0 - NHI + 2 * it) * P, P)], P)
            head_of(NSEQ - 1)

        @block.vector
        def _(dve):
            def statistics(n):
                r = size(n)
                dve.wait_ge(x_done[n], 16 if n < NB - 1 else 32)
                nc.vector.bn_stats(stats[0:r, n, :], x_in[0:r, n % 2, :]).then_inc(stats_ready, 1)

            def mean_and_variance(n):
                r = size(n)
                dve.wait_ge(stats_ready, n + 1)
                nc.vector.bn_aggr(moments[0:r, n, :], stats[0:r, n, :]).then_inc(moments_ready, 1)

            def variance(n):
                r = size(n)
                dve.wait_ge(moments_ready, n + 1)
                nc.vector.tensor_scalar(base[0:r, n, 0:1], moments[0:r, n, 1:2], EPS, None,
                                        ALU.add).then_inc(var_ready, 1)

            def centre(n):
                r = size(n)
                dve.wait_ge(moments_ready, n + 1)
                nc.vector.tensor_scalar(xr[0:r, n % 2, :], x_in[0:r, n % 2, :], moments[0:r, n, 0:1], 0.0,
                                        ALU.subtract, ALU.max).then_inc(xr_ready, 1)

            def add_group(n, _, q, a, b):
                r = size(n)
                dve.wait_ge(row_stored, q + 1)
                dve.wait_ge(col_transposed, BELOW[q + 1])
                if a == n:
                    diag = S_blocks(n, n, n + 1)[0:r]
                    nc.vector.scalar_tensor_tensor(out=diag, in0=ident[0:r, 0:r], scalar=2.0, in1=diag,
                                                   op0=ALU.mult, op1=ALU.add).then_inc(eye_added, 1)
                    dve.wait_ge(eye_added, n + 1)
                blocks = S_blocks(n, a, b)[0:r]
                if b <= LO and n > 0:
                    last = nc.vector.tensor_tensor(blocks, blocks, AT[0:r, n, a * P:end(b)], ALU.add)
                else:
                    part = 1 + q - LOW[n] if n > 0 else q
                    last = nc.vector.scalar_tensor_tensor(out=blocks, in0=blocks, scalar=1.0,
                                                          in1=AT[0:r, n, a * P:end(b)], op0=ALU.mult, op1=ALU.add,
                                                          accum_out=sums[0:r, n, part:part + 1])
                last.then_inc(row_added, 1)

            def degrees(n):
                r = size(n)
                if 0 < n < NB - 1:
                    dve.wait_ge(heads, step_chunk(n) + 1)
                dve.wait_ge(row_added, FIRST[n + 1])
                if n > LO:
                    dve.wait_ge(sums_ready, n - LO + (n > SUM_STEP))
                nc.vector.reduce_sum(degree[0:r, n:n + 1], sums[0:r, n, 0:PARTS[n]], AX.X).then_inc(degree_ready, 1)
                dve.wait_ge(degree_ready, n + 1)
                nc.vector.tensor_scalar(positive[0:r, n:n + 1], degree[0:r, n:n + 1], 0.0, None, ALU.is_gt)
                nc.vector.tensor_scalar(base[0:r, n, 1:2], degree[0:r, n:n + 1], 0.5, TINY,
                                        ALU.mult, ALU.max).then_inc(base_ready, 1)

            def mixed_tail(dst, head, source):
                return nc.vector.scalar_tensor_tensor(out=dst, in0=head, scalar=minus_rests[0:MIX, :], in1=source,
                                                      op0=ALU.mult, op1=ALU.add)

            def rest_lo(n):
                c = step_chunk(n)
                dve.wait_ge(heads, c + 1)
                if n < NB - 1:
                    nc.vector.tensor_tensor(ring[:, c % SLOTS, 1, :], A_lo[:, n, :],
                                            ring[:, c % SLOTS, 0, :].bitcast(f32), ALU.subtract).then_inc(rests, 1)
                else:
                    mixed_tail(ring[0:MIX, c % SLOTS, 1, :], ring[0:MIX, c % SLOTS, 0, :].bitcast(f32),
                               A_lo[0:MIX, Y, :]).then_inc(rests, 1)

            def scale_g(n):
                r = size(n)
                dve.wait_ge(power_ready, n + 1)
                dve.wait_ge(base_ready, n + 1)
                nc.vector.tensor_scalar(g_scale[0:r, n:n + 1], power[0:r, n, 1:2], positive[0:r, n:n + 1],
                                        power[0:r, n, 0:1], ALU.mult, ALU.mult).then_inc(scale_ready, 1)

            def rest_g(n):
                r = size(n)
                dve.wait_ge(g_head, n + 1)
                dst = g[0:r, n, 1, :] if n < NB - 1 else rest_tail[0:TAIL, :]
                nc.vector.scalar_tensor_tensor(out=dst, in0=xr[0:r, n % 2, :],
                                               scalar=g_scale[0:r, n:n + 1], in1=g[0:r, n, 0, :].bitcast(f32),
                                               op0=ALU.mult, op1=ALU.subtract).then_inc(g_ready, 1)

            def rest_half(c, slot, half, source, cols):
                k0, k1 = HALVES[half]
                dve.wait_ge(heads, c + 1)
                v = ring[:, slot, :, 0:(k1 - k0) * P].rearrange("p t (k c) -> p t k c", c=P)
                kf = min(k1, NB - 1)
                last = nc.vector.tensor_tensor(v[:, 1, 0:kf - k0, 0:cols], source(slice(k0, kf), P),
                                               v[:, 0, 0:kf - k0, 0:cols].bitcast(f32), ALU.subtract)
                if k1 == NB:
                    last = mixed_tail(v[0:MIX, 1, kf - k0, 0:cols], v[0:MIX, 0, kf - k0, 0:cols].bitcast(f32),
                                      source(Y, MIX))
                last.then_inc(rests, 1)

            def rest_of(s, halves=(0, 1)):
                for half in halves:
                    rest_half(chunk(s, half), slots_of(s)[half], half, *column(s))

            def add_groups(n, j0, j1):
                for group in groups_of(n)[j0:j1]:
                    add_group(*group)

            dve.wait_ge(ident_ready, 1)
            dve.wait_ge(minus_ready, 1)
            add_groups(0, 0, 2)
            statistics(0)
            add_groups(0, 2, 3)
            mean_and_variance(0)
            add_groups(0, 3, 4)
            variance(0)
            degrees(0)
            centre(0)
            rest_lo(0)
            scale_g(0)
            rest_g(0)
            statistics(1)
            add_groups(1, 0, 4)
            mean_and_variance(1)
            variance(1)
            centre(1)
            for n in range(1, MANY + 1):
                degrees(n)
                rest_lo(n)
                scale_g(n)
                add_groups(n + 1, 0, 1)
                rest_g(n)
                add_groups(n + 1, 1, 2)
                statistics(n + 1)
                add_groups(n + 1, 2, 3)
                mean_and_variance(n + 1)
                add_groups(n + 1, 3, 4)
                variance(n + 1)
                centre(n + 1)
            for n in range(MANY + 1, NB - 1):
                degrees(n)
                statistics(n + 1)
                scale_g(n)
                rest_lo(n)
                rest_g(n)
                add_groups(n + 1, 0, 1)
                mean_and_variance(n + 1)
                add_groups(n + 1, 1, 2)
                variance(n + 1)
                centre(n + 1)
            degrees(NB - 1)
            rest_of(0, (0,))
            scale_g(NB - 1)
            rest_lo(NB - 1)
            rest_g(NB - 1)

            nc.vector.scalar_tensor_tensor(out=z_scale[:, 0:NB - 1], in0=power[:, 0:NB - 1, 1], scalar=0.5,
                                           in1=positive[:, 0:NB - 1], op0=ALU.mult, op1=ALU.mult)
            nc.vector.scalar_tensor_tensor(out=z_scale[0:TAIL, NB - 1:], in0=power[0:TAIL, NB - 1:, 1], scalar=0.5,
                                           in1=positive[0:TAIL, NB - 1:], op0=ALU.mult,
                                           op1=ALU.mult).then_inc(z_scale_ready, 1)

            def z_rest(i, src, so_far):
                r = size(i)
                dst = z[0:r, i, 1, :]
                if i == NB - 1:
                    dve.wait_ge(tail_g_done, 32)
                    dst = rest_tail[0:r, :]
                dve.wait_ge(z_head, so_far)
                last = nc.vector.scalar_tensor_tensor(out=dst, in0=src[0:r, :],
                                                      scalar=z_scale[0:r, i:i + 1],
                                                      in1=z[0:r, i, 0, :].bitcast(f32),
                                                      op0=ALU.mult, op1=ALU.subtract)
                return last

            rest_of(0, (1,))
            rest_of(1)
            for i in range(LO):
                z_rest(i, bank[i], i + 1)
            for s in range(2, 2 + NHI):
                rest_of(s)
                z_rest(SECOND[s - 2], bank[6 + (s - 2) % 2],
                       LO + s - 1 + (s - 2 >= TAIL_AT)).then_inc(drained, 1)
            dve.wait_ge(res_done, 48)

            def result(m, slot, r=P):
                dst = y_out[0:r, bass.ds(m, 1), :].rearrange("p o d -> p (o d)")
                res = x_res[0:r, bass.ds(m, 1), :].rearrange("p o d -> p (o d)")
                nc.vector.tensor_tensor(dst, bank[slot][0:r, :], res,
                                        ALU.add).then_inc(drained, 1)

            with dve.Fori(0, (NSEQ - 1 - (2 + NHI)) // 2) as it:
                for odd in range(2):
                    s0 = 2 + NHI + odd
                    for half in range(2):
                        rest_half(chunk(s0, half) + 4 * it, slots_of(s0)[half], half,
                                  lambda ks, r: AT[0:r, ks, bass.ds((s0 - NHI + 2 * it) * P, P)], P)
                    dve.wait_ge(chunk_used, chunk(s0 - 2, 2) + 4 * it)
                    result(odd + 2 * it, 6 + (s0 - 2) % 2)
            rest_of(NSEQ - 1)
            for s in range(NSEQ - 3, NSEQ):
                dve.wait_ge(chunk_used, chunk(s, 2))
                result(s - NHI, 6 + s % 2, size(s - NHI))

        @block.tensor
        def _(pe):
            def groups_stored(q):
                pe.wait_ge(row_stored, q)
                pe.wait_ge(col_stored, BELOW[q])

            def transpose_for_row(n, _, q, a, b):
                before = q if q >= EARLY else q - 3
                if before > 0:
                    pe.wait_ge(row_stored, before)
                if b <= LO:
                    pe.wait_ge(load_lo[n], 16 * len(loads_lo(n)))
                elif n < NB - 1:
                    pe.wait_ge(load_hi[n], 16 * len(loads_hi(n)))
                if n == 0:
                    pe.wait_ge(first_lo, 16)
                for i in range(a, b):
                    o = (i - a) * P
                    last = nc.tensor.transpose(group_banks(q)[0][0:size(n), o:o + size(i)],
                                               S_blocks(i, n, n + 1)[0:size(i)], ident[0:size(i), 0:size(i)])
                last.then_inc(row_transposed, 1)

            def transpose_for_column(n, _, q, a, b):
                before = q if q >= EARLY else q - 3
                r = size(n)
                if max(a, n + 1) >= b:
                    return
                if before > 0:
                    pe.wait_ge(col_stored, BELOW[before])
                if n == 0:
                    pe.wait_ge(first_lo if b <= LO else first_hi, 16)
                for i in range(max(a, n + 1), b):
                    o = (i - a) * P
                    last = nc.tensor.transpose(group_banks(q)[1][0:size(i), o:o + r], S_blocks(n, i, i + 1)[0:r],
                                               ident[0:r, 0:r])
                last.then_inc(col_transposed, 1)

            def transpose_group(*group):
                transpose_for_row(*group)
                transpose_for_column(*group)

            def product(dst, slot, b, m, rhs, r, parts, first, final):
                stationary = ring[0:r, slot, parts[0], b * P:b * P + m]
                return nc.tensor.matmul(dst, stationary, rhs[0:r, parts[1], :], start=first, stop=final)

            pe.wait_ge(ident_ready, 1)
            for two in (groups_of(0)[:2], groups_of(0)[2:]):
                for group in two:
                    transpose_for_column(*group)
                for group in two:
                    transpose_for_row(*group)
            for group in groups_of(1):
                transpose_group(*group)

            def step(k):
                c = step_chunk(k)
                if k == 0:
                    todo = dict(zip(LATE, groups_of(2)))
                elif k + 2 < NB:
                    todo = dict(zip(PLACES[len(groups_of(k + 2))], groups_of(k + 2)))
                else:
                    todo = {}
                if k == 0:
                    order = [(i, *parts) for parts in ((0, 0), (1, 0), (0, 1)) for i in range(LO)]
                    pe.wait_ge(heads, 1)
                    pe.wait_ge(g_head, 1)
                elif k < NB - 1:
                    order = [(i, *parts) for i in range(LO) for parts in ((0, 0), (0, 1), (1, 0))]
                    pe.wait_ge(rests, c + 1)
                    pe.wait_ge(g_ready, k + 1)
                else:
                    order = [(i, *parts) for i in range(LO) for parts in ((0, 0), (1, 1))]
                    pe.wait_ge(rests, c + 1)
                    pe.wait_ge(g_head, NB + 1)
                    pe.wait_ge(tail_g_done, 32)
                seen = [0] * LO
                for at_product, (i, part, g_part) in enumerate(order):
                    if k == 0 and at_product == LO:
                        pe.wait_ge(rests, 1)
                    if k == 0 and at_product == 2 * LO:
                        pe.wait_ge(g_ready, 1)
                    if k == 0 and (part, g_part) == (0, 0):
                        groups_stored(LAST_IN[i // 2] + 1)
                    rows = MIX if k == NB - 1 and part == 1 else P
                    last = product(bank[i][:, :], c % SLOTS, i, P, g[:, k], rows, (part, g_part),
                                   k == 0 and seen[i] == 0, k == NB - 1 and seen[i] == 1)
                    seen[i] += 1
                    if at_product == len(order) - 1:
                        last.then_inc(chunk_used, 1)
                    if at_product in todo:
                        transpose_group(*todo[at_product])

            def output_half(c, slot, half, acc, m, operand):
                pe.wait_ge(rests, c + 1)
                for k in range(*HALVES[half]):
                    if k < NB - 1:
                        if operand is z and k == NB - 2:
                            pe.wait_ge(drained, NHI)
                        for parts in ((0, 0), (0, 1), (1, 0)):
                            last = product(bank[acc][0:m, :], slot, k - HALVES[half][0], m, operand[:, k], P,
                                           parts, k == 0 and parts == (0, 0), False)
                    else:
                        if operand is z:
                            pe.wait_ge(tail_z_done, 32)
                        for parts, rows in (((0, 0), P), ((1, 1), MIX)):
                            last = product(bank[acc][0:m, :], slot, k - HALVES[half][0], m, operand[:, k], rows,
                                           parts, False, parts == (1, 1))
                last.then_inc(chunk_used, 1)

            for k in range(NB - 1):
                step(k)

            groups_stored(NQ)
            for s in range(NHI):
                for half in range(2):
                    if s >= 2 and half == 0:
                        pe.wait_ge(drained, s - 1)
                    output_half(chunk(s, half), slots_of(s)[half], half, 6 + s % 2, size(SECOND[s]), g)
                    if s == half == 0:
                        step(NB - 1)

            pe.wait_ge(drained, NHI - 1)
            with pe.Fori(0, (NB - 1) // 2) as it:
                for odd in range(2):
                    s0 = NHI + odd
                    pe.wait_ge(drained, s0 - 1 + 2 * it)
                    for half in range(2):
                        output_half(chunk(s0, half) + 4 * it, slots_of(s0)[half], half, 6 + s0 % 2, P, z)
            pe.wait_ge(drained, NSEQ - 2)
            for half in range(2):
                output_half(chunk(NSEQ - 1, half), slots_of(NSEQ - 1)[half], half, 6 + (NSEQ - 1) % 2, TAIL, z)


def kernel(x, adj):
    import numpy as np
    import concourse.bacc as bacc
    from concourse.bass_utils import run_bass_kernel_spmd

    nc = bacc.Bacc("TRN2", target_bir_lowering=False, num_devices=1)
    arrays, args = {}, []
    for name, a in (("x", x), ("adj", adj)):
        a = np.ascontiguousarray(a)
        arrays[f"in_{name}_dram"] = a
        args.append(nc.dram_tensor(f"in_{name}_dram", a.shape, mybir.dt.from_np(a.dtype), kind="ExternalInput").ap())
    shape = arrays["in_x_dram"].shape
    args.append(nc.dram_tensor("out_dram", shape, mybir.dt.float32, kind="ExternalOutput").ap())
    graph_layer(nc, *args)
    r = run_bass_kernel_spmd(nc, [arrays], core_ids=[0])
    return r.results[0]["out_dram"]
```
